# Optimizing a Trainium2 kernel written in Bass

```python
import numpy as np
import jax
import jax.numpy as jnp

def _softmax(x, axis=-1):
    return jax.nn.softmax(x, axis=axis)

def _gelu(x):
    return jax.nn.gelu(x, approximate=True)

def _silu(x):
    return jax.nn.silu(x)

def _sigmoid(x):
    return jax.nn.sigmoid(x)

def _layernorm(x, axis=-1, eps=1e-05):
    m = jnp.mean(x, axis=axis, keepdims=True)
    v = jnp.var(x, axis=axis, keepdims=True)
    return (x - m) / jnp.sqrt(v + eps)

def _scatter_add(tgt, idx, src, axis=0):
    return tgt.at[idx].add(src)

def _segment_sum(src, seg, n):
    return jax.ops.segment_sum(src, seg, n)
kernel_name = 'mk_rec_standalone_d1_rec_r8_596371'

def setup_inputs(seed: int=0):
    np.random.seed(seed)
    _w = jnp.asarray

    def _rec_inputs():
        import jax
        import jax.numpy as jnp
        _rk = jax.random.key(seed)
        r_state = -0.000928989 + 1.00043 * jax.random.normal(jax.random.fold_in(_rk, 1), (2048, 256), jnp.float32)
        r_token = jax.random.randint(jax.random.fold_in(_rk, 2), (2048,), 49, 31986, jnp.int32)
        return (r_state, r_token)
    r_state, r_token = _rec_inputs()

    def _L0_rec_setup():
        import jax, jax.numpy as jnp
        import numpy as np
        VOCAB = 4000
        HIDDEN = 256
        NLAYERS = 6
        BATCH = 512
        key = jax.random.key(seed)
        k1, k2, k3, k4 = jax.random.split(key, 4)
        state = jax.random.normal(k1, (BATCH, HIDDEN), dtype=jnp.float32)
        token = jax.random.randint(k2, (BATCH,), 0, VOCAB, dtype=jnp.int32)
        ih = jax.random.normal(k3, (NLAYERS, VOCAB, HIDDEN), dtype=jnp.float32) * 0.02
        hh = jax.random.normal(k4, (NLAYERS, HIDDEN, HIDDEN), dtype=jnp.float32) * 0.02
        return {'state': state, 'token': token, 'ih': ih, 'hh': hh}
    _L0_rec_all = _L0_rec_setup()
    _L0_rec_in = {k: v for k, v in _L0_rec_all.items() if k in ('ih', 'hh')}
    del _L0_rec_all
    return {'r_state': r_state, 'r_token': r_token, 'L0_rec_ih': _L0_rec_in['ih'], 'L0_rec_hh': _L0_rec_in['hh']}

def reference(r_state, r_token, L0_rec_ih, L0_rec_hh):
    import jax
    import jax.numpy as jnp

    def _L0_rec_ref(state, token, ih, hh):
        import jax, jax.numpy as jnp
        import numpy as np
        VOCAB = 4000
        HIDDEN = 256
        NLAYERS = 6
        BATCH = 512
        n_layers = ih.shape[0]
        for i in range(n_layers):
            gate = ih[i][token]
            state = jnp.tanh(state + jnp.matmul(state, hh[i]) * gate)
        return state
    y = _L0_rec_ref(r_state, r_token, L0_rec_ih, L0_rec_hh)
    return y

_drawn_inputs = setup_inputs


def setup_inputs(seed=0):
    import zlib

    import numpy as np

    out = dict(_drawn_inputs(seed))
    spreads = {}
    factors = {'L0_rec_ih': 3.854, 'L0_rec_hh': 3.835}
    for name, (base, spread) in spreads.items():
        noise = np.random.default_rng([zlib.crc32(name.encode()), seed]).standard_normal(out[name].shape)
        drawn = base * np.exp(spread * noise) if base else spread * noise
        out[name] = jnp.asarray(drawn.astype(out[name].dtype))
    for name, factor in factors.items():
        out[name] = (out[name] * factor).astype(out[name].dtype)
    return out
```

```python
import concourse.bass as bass
from concourse import mybir
from contextlib import ExitStack


def gated_recurrence(nc, state_rows, state_cols, token, gates_first, gates_mid, gates_late, weights, out):
    fp32, fp16 = mybir.dt.float32, mybir.dt.float16
    i32, u32 = mybir.dt.int32, mybir.dt.uint32
    ALU = mybir.AluOpType
    ACT = mybir.ActivationFunctionType

    P = 128
    ROWS, HID = state_rows.shape
    LAYERS = weights.shape[0]
    VOCAB = gates_mid.shape[0]
    TILES = ROWS // P
    PAIR = 2
    PAIRS = TILES // PAIR
    KC = HID // P
    WIDE = PAIR * HID
    CHUNKS = [(0, 1), (1, 3), (3, LAYERS)]
    TABLES = [gates_first, gates_mid, gates_late]
    LAST = LAYERS - 1
    LOOPS = [(1, 3), (3, LAST)]
    LAG = 3
    NMM, NTR, NU = 4, 2, 4
    POOL_ADDS = {3: (0, 1, 2, 3, 4, 5, 6, 7), LAST: (0, 2, 4, 6)}
    SPLIT = LAYERS - 1
    TOP = 14
    STATE_SCALE = float(2 ** 15)
    MANTISSA, BIAS = 23, 127

    def pool_adds(layer):
        for first, chosen in POOL_ADDS.items():
            if layer == first or (first < LAST and first <= layer < LAST):
                return chosen
        return ()

    with ExitStack() as ctx:
        def sb(name, shape, dt):
            return ctx.enter_context(nc.sbuf_tensor(name, shape, dt))

        def sem(name):
            return ctx.enter_context(nc.semaphore(name))

        state = sb("state", [P, TILES, HID], fp32)
        first_cols = sb("first_cols", [P, KC, ROWS], fp32)
        head = sb("head", [P, PAIRS, KC, PAIR * P], fp16)
        rest = sb("rest", [P, PAIRS, KC, PAIR * P], fp16)
        gates = sb("gates", [P, TILES, LAYERS, HID], fp32)
        sums = sb("sums", [P, NU, PAIR, HID], fp32)
        w_full = sb("w_full", [P, LAYERS, KC * HID], fp32)
        w_head = sb("w_head", [P, SPLIT, KC * HID], fp16)
        w_rest = sb("w_rest", [P, SPLIT, KC * HID], fp16)
        w_abs = sb("w_abs", [P, KC * HID], fp32)
        w_sum = sb("w_sum", [P, SPLIT], fp32)
        w_total = sb("w_total", [P, SPLIT], fp32)
        w_expo = sb("w_expo", [P, SPLIT], i32)
        w_up = sb("w_up", [P, SPLIT], i32)
        w_down = sb("w_down", [P, SPLIT], i32)
        ones = sb("ones", [P, P], fp32)
        ident = sb("ident", [P, P], fp32)
        tok = sb("tok", [P, TILES], i32)
        wrap = sb("wrap", [P, TILES], fp32)
        tok_wrapped = sb("tok_wrapped", [P, TILES], fp32)
        index = sb("index", [P, TILES], u32)

        products = [ctx.enter_context(nc.psum_tensor(f"products{i}", [P, PAIR, HID], fp32)) for i in range(NMM)]
        turned = [ctx.enter_context(nc.psum_tensor(f"turned{i}", [P, KC, PAIR * P], fp32)) for i in range(NTR)]
        totals = ctx.enter_context(nc.psum_tensor("totals", [P, SPLIT], fp32))

        tok_in = sem("tok_in")
        w_first_in = sem("w_first_in")
        w_split_in = sem("w_split_in")
        cols_in = [sem(f"cols_in{q}") for q in range(PAIRS)]
        rows_in = [sem(f"rows_in{q}") for q in range(PAIRS)]
        gates_in = [[sem(f"gates{c}_in{q}") for q in range(PAIRS)] for c in range(len(CHUNKS))]
        ident_zero = sem("ident_zero")
        ident_ready = sem("ident_ready")
        ones_ready = sem("ones_ready")
        index_steps = sem("index_steps")
        scale_steps = sem("scale_steps")
        w_sum_ready = sem("w_sum_ready")
        total_ready = sem("total_ready")
        w_head_ready = sem("w_head_ready")
        w_rest_ready = sem("w_rest_ready")
        product_ready = sem("product_ready")
        gated_ready = sem("gated_ready")
        vector_added = sem("vector_added")
        pool_added = sem("pool_added")
        state_ready = sem("state_ready")
        turned_ready = sem("turned_ready")
        head_ready = sem("head_ready")
        rest_ready = sem("rest_ready")
        stored = sem("stored")

        INDEX_STEPS = 3
        SCALE_STEPS = 4

        def pair_rows(t, q):
            return t[:, PAIR * q:PAIR * (q + 1), :]

        block = ctx.enter_context(nc.Block())

        class Layer:
            def __init__(self, at, low):
                self.at, self.low = at, low

            def count(self, per_layer, before):
                return self.at * per_layer + before

            def adds(self, q, pool):
                def made(l, upto=PAIRS):
                    return sum((p in pool_adds(l)) == pool for p in range(upto))
                base = sum(made(l) for l in range(self.low))
                here = made(self.low, q + 1)
                if isinstance(self.at, int):
                    return base + here
                return self.at * made(self.low) + (base - self.low * made(self.low) + here)

        def layers(eng, step):
            step(Layer(0, 0))
            for lo, hi in LOOPS:
                with eng.Fori(lo, hi) as at:
                    step(Layer(at, lo))
            step(Layer(LAST, LAST))

        @block.sync
        def _(sp):
            sp.dma_start(tok[:, :], token.rearrange("(p t) -> p t", t=TILES)).then_inc(tok_in, 16)
            sp.dma_start(w_full[:, 0, :].rearrange("p (c n) -> p c n", c=KC),
                         weights[0].rearrange("(c p) n -> p c n", c=KC)).then_inc(w_first_in, 16)
            rows_v = state_rows.rearrange("(p t) h -> p t h", t=TILES)
            cols_v = state_cols.rearrange("(c k) r -> k c r", c=KC)
            for q in range(PAIRS):
                cols = slice(q * PAIR * P, (q + 1) * PAIR * P)
                sp.dma_start(first_cols[:, :, cols], cols_v[:, :, cols]).then_inc(cols_in[q], 16)
                sp.dma_start(pair_rows(state, q), pair_rows(rows_v, q)).then_inc(rows_in[q], 16)
                if q == 1:
                    for l in range(1, LAYERS):
                        sp.dma_start(w_full[:, l, :].rearrange("p (c n) -> p c n", c=KC),
                                     weights[l].rearrange("(c p) n -> p c n", c=KC)).then_inc(w_split_in, 16)
            out_v = out.rearrange("(p t) h -> p t h", t=TILES)
            for q in range(PAIRS):
                sp.wait_ge(state_ready, LAST * PAIRS + q + 1)
                sp.dma_start(pair_rows(out_v, q), pair_rows(state, q)).then_inc(stored, 16)
            sp.wait_ge(stored, 16 * PAIRS)

        @block.gpsimd
        def _(pool):
            nc.gpsimd.memset(ident[:, :], 0.0).then_inc(ident_zero, 1)
            nc.gpsimd.memset(ones[:, :], 1.0).then_inc(ones_ready, 1)
            pool.wait_ge(ident_zero, 1)
            nc.gpsimd.affine_select(out=ident[:, :], in_=ident[:, :], compare_op=ALU.not_equal, fill=1.0,
                                    base=0, pattern=[[-1, P]], channel_multiplier=1).then_inc(ident_ready, 1)
            pool.wait_ge(index_steps, INDEX_STEPS)
            for c, (lo, hi) in enumerate(CHUNKS):
                for t in range(TILES):
                    pool.indirect_dma_start(
                        gates[:, t, lo:hi, :].rearrange("p l h -> p (l h)"), None, TABLES[c],
                        bass.IndirectOffsetOnAxis(ap=index[:, t:t + 1], axis=0),
                    ).then_inc(gates_in[c][t // PAIR], 16)

            def step(layer):
                for q in pool_adds(layer.low):
                    pool.wait_ge(gated_ready, layer.count(PAIRS, q + 1))
                    nc.gpsimd.tensor_tensor(sums[:, q % NU], sums[:, q % NU], pair_rows(state, q),
                                            ALU.add).then_inc(pool_added, 1)

            for lo, hi in LOOPS:
                if pool_adds(lo):
                    with pool.Fori(lo, hi) as at:
                        step(Layer(at, lo))
            step(Layer(LAST, LAST))

        @block.tensor
        def _(pe):
            def product(layer, q):
                bank = products[q % NMM]
                if layer.low == 0:
                    pe.wait_ge(cols_in[q], 16)
                    if q == 0:
                        pe.wait_ge(w_first_in, 16)
                else:
                    pe.wait_ge(rest_ready, layer.count(PAIRS, q + 1 - PAIRS))
                if layer.low > 0 or q >= NMM:
                    pe.wait_ge(gated_ready, layer.count(PAIRS, q + 1 - NMM))
                for j in range(PAIR):
                    if layer.low == 0:
                        for k in range(KC):
                            cols = (PAIR * q + j) * P
                            last = nc.tensor.matmul(bank[:, j, :], first_cols[:, k, cols:cols + P],
                                                    w_full[:, 0, k * HID:(k + 1) * HID],
                                                    start=(k == 0), stop=(k == KC - 1))
                        continue
                    terms = [(s, w, k) for k in range(KC) for s, w in ((head, w_head), (head, w_rest), (rest, w_head))]
                    for n, (s, w, k) in enumerate(terms):
                        cut = bass.ds((layer.at - 1) * (KC * HID) + k * HID, HID)
                        last = nc.tensor.matmul(bank[:, j, :], s[:, q, k, j * P:(j + 1) * P],
                                                w[:, :, :].rearrange("p l n -> p (l n)")[:, cut],
                                                start=(n == 0), stop=(n == len(terms) - 1))
                last.then_inc(product_ready, 1)

            def turn(layer, q):
                pe.wait_ge(state_ready, layer.count(PAIRS, q + 1))
                if layer.low > 0 or q >= NTR:
                    pe.wait_ge(rest_ready, layer.count(PAIRS, q + 1 - NTR))
                for j in range(PAIR):
                    for k in range(KC):
                        last = nc.tensor.transpose(turned[q % NTR][:, k, j * P:(j + 1) * P],
                                                   state[:, PAIR * q + j, k * P:(k + 1) * P], ident[:, :])
                last.then_inc(turned_ready, 1)

            pe.wait_ge(ident_ready, 1)

            def step(layer):
                for q in range(PAIRS):
                    product(layer, q)
                    if q >= LAG and layer.low < LAST:
                        turn(layer, q - LAG)
                    elif q < LAG and layer.low > 0:
                        turn(Layer(layer.at - 1, max(layer.low - 1, 0)), PAIRS + q - LAG)
                    if layer.low == 0 and q == 5:
                        pe.wait_ge(ones_ready, 1)
                        pe.wait_ge(w_sum_ready, SPLIT)
                        nc.tensor.matmul(totals[:, :], ones[:, :], w_sum[:, :],
                                         start=True, stop=True).then_inc(total_ready, 1)
                if layer.low == 0:
                    pe.wait_ge(w_rest_ready, SPLIT)

            layers(pe, step)

        @block.scalar
        def _(act):
            def make_head(layer, q):
                act.wait_ge(turned_ready, layer.count(PAIRS, q + 1))
                nc.scalar.activation(head[:, q], turned[q % NTR][:, :, :], ACT.Copy,
                                     scale=STATE_SCALE).then_inc(head_ready, 1)

            def new_state(layer, q):
                if q in pool_adds(layer.low):
                    act.wait_ge(pool_added, layer.adds(q, True))
                else:
                    act.wait_ge(vector_added, layer.adds(q, False))
                nc.scalar.activation(pair_rows(state, q), sums[:, q % NU], ACT.Tanh).then_inc(state_ready, 1)

            def step(layer):
                for q in range(PAIRS):
                    if q >= LAG and layer.low < LAST:
                        make_head(layer, q - LAG)
                    elif q < LAG and layer.low > 0:
                        make_head(Layer(layer.at - 1, max(layer.low - 1, 0)), PAIRS + q - LAG)
                    new_state(layer, q)
                    if layer.low == 0 and q < SPLIT:
                        if q == 0:
                            act.wait_ge(w_split_in, 16 * SPLIT)
                        if q >= 1:
                            act.wait_ge(w_sum_ready, q)
                        nc.scalar.activation(w_abs[:, :], w_full[:, 1 + q, :], ACT.Abs,
                                             accum_out=w_sum[:, q:q + 1]).then_inc(w_sum_ready, 1)
                    if layer.low == 0 and q == PAIRS - 1:
                        act.wait_ge(scale_steps, SCALE_STEPS)
                        for l in range(SPLIT):
                            nc.scalar.activation(w_head[:, l, :], w_full[:, 1 + l, :], ACT.Copy,
                                                 scale=w_up[:, l:l + 1].bitcast(fp32)).then_inc(w_head_ready, 1)

            layers(act, step)

        @block.vector
        def _(dve):
            dve.wait_ge(tok_in, 16)
            nc.vector.tensor_scalar(wrap[:, :], tok[:, :], 0.0, float(VOCAB), ALU.is_lt,
                                    ALU.mult).then_inc(index_steps, 1)
            dve.wait_ge(index_steps, 1)
            nc.vector.tensor_tensor(tok_wrapped[:, :], tok[:, :], wrap[:, :], ALU.add).then_inc(index_steps, 1)
            dve.wait_ge(index_steps, 2)
            nc.vector.tensor_scalar(index[:, :], tok_wrapped[:, :], 0.0, float(VOCAB - 1), ALU.max,
                                    ALU.min).then_inc(index_steps, 1)

            def gated(layer, q):
                dve.wait_ge(product_ready, layer.count(PAIRS, q + 1))
                chunk = [c for c, (lo, hi) in enumerate(CHUNKS) if lo <= layer.low < hi][0]
                dve.wait_ge(gates_in[chunk][q], 16 * PAIR)
                if layer.low > 0 or q >= NU:
                    dve.wait_ge(state_ready, layer.count(PAIRS, q + 1 - NU))
                g = gates[:, PAIR * q:PAIR * (q + 1), layer.at, :] if isinstance(layer.at, int) else \
                    gates[:, PAIR * q:PAIR * (q + 1), :, :].rearrange("p t l h -> p t (l h)")[:, :, bass.ds(layer.at * HID, HID)]
                if layer.low == 0:
                    nc.vector.tensor_tensor(sums[:, q % NU], products[q % NMM][:, :, :], g,
                                            ALU.mult).then_inc(gated_ready, 1)
                else:
                    down = w_down[:, :].bitcast(fp32)[:, bass.ds(layer.at - 1, 1)]
                    nc.vector.scalar_tensor_tensor(out=sums[:, q % NU], in0=products[q % NMM][:, :, :], scalar=down,
                                                   in1=g, op0=ALU.mult, op1=ALU.mult).then_inc(gated_ready, 1)

            def add_state(layer, q):
                dve.wait_ge(gated_ready, layer.count(PAIRS, q + 1))
                if layer.low == 0:
                    dve.wait_ge(rows_in[q], 16)
                nc.vector.tensor_tensor(sums[:, q % NU], sums[:, q % NU], pair_rows(state, q),
                                        ALU.add).then_inc(vector_added, 1)

            def make_rest(layer, q):
                dve.wait_ge(head_ready, layer.count(PAIRS, q + 1))
                nc.vector.scalar_tensor_tensor(out=rest[:, q], in0=turned[q % NTR][:, :, :], scalar=STATE_SCALE,
                                               in1=head[:, q], op0=ALU.mult,
                                               op1=ALU.subtract).then_inc(rest_ready, 1)

            REST_LAG = LAG + 1

            def scales():
                dve.wait_ge(total_ready, 1)
                nc.vector.tensor_scalar(w_total[:, :], totals[:, :], 2.0 ** -90, None,
                                        ALU.max).then_inc(scale_steps, 1)
                dve.wait_ge(scale_steps, 1)
                nc.vector.tensor_scalar(w_expo[:, :], w_total[:, :].bitcast(i32), 0x7F800000, None,
                                        ALU.bitwise_and).then_inc(scale_steps, 1)
                dve.wait_ge(scale_steps, 2)
                nc.vector.tensor_scalar(w_up[:, :], w_expo[:, :], -1.0, float((2 * BIAS + TOP) << MANTISSA),
                                        ALU.mult, ALU.add).then_inc(scale_steps, 1)
                nc.vector.tensor_scalar(w_down[:, :], w_expo[:, :], -float((TOP + 15) << MANTISSA), None,
                                        ALU.add).then_inc(scale_steps, 1)

            def step(layer):
                for q in range(PAIRS):
                    gated(layer, q)
                    if q >= REST_LAG and layer.low < LAST:
                        make_rest(layer, q - REST_LAG)
                    elif q < REST_LAG and layer.low > 0:
                        make_rest(Layer(layer.at - 1, max(layer.low - 1, 0)), PAIRS + q - REST_LAG)
                    if q not in pool_adds(layer.low):
                        add_state(layer, q)
                    if layer.low == 0 and q == 6:
                        scales()
                    if layer.low == 0 and q == PAIRS - 1:
                        dve.wait_ge(scale_steps, SCALE_STEPS)
                        for l in range(SPLIT):
                            dve.wait_ge(w_head_ready, l + 1)
                            nc.vector.scalar_tensor_tensor(
                                out=w_rest[:, l, :], in0=w_full[:, 1 + l, :], scalar=w_up[:, l:l + 1].bitcast(fp32),
                                in1=w_head[:, l, :], op0=ALU.mult, op1=ALU.subtract).then_inc(w_rest_ready, 1)

            layers(dve, step)


def kernel(**inputs):
    import numpy as _np
    import concourse.bacc as _bacc
    from concourse import mybir as _mybir
    from concourse.bass_utils import run_bass_kernel_spmd as _run

    state = _np.asarray(inputs["r_state"])
    token = _np.asarray(inputs["r_token"])
    ih = _np.asarray(inputs["L0_rec_ih"])
    hh = _np.asarray(inputs["L0_rec_hh"])
    rows, hid = state.shape
    layers, vocab, _ = ih.shape

    def together(lo, hi):
        return ih[lo:hi].transpose(1, 0, 2).reshape(vocab, (hi - lo) * hid)

    host = {
        "state_rows": state,
        "state_cols": state.reshape(128, rows // 128, hid).transpose(2, 1, 0).reshape(hid, rows),
        "token": token,
        "gates_first": together(0, 1),
        "gates_mid": together(1, 3),
        "gates_late": together(3, layers),
        "weights": hh,
    }
    nc = _bacc.Bacc("TRN2", target_bir_lowering=False, num_devices=1)
    arrays, args = {}, []
    for name, a in host.items():
        a = _np.ascontiguousarray(a)
        arrays[f"in_{name}"] = a
        args.append(nc.dram_tensor(f"in_{name}", a.shape, _mybir.dt.from_np(a.dtype), kind="ExternalInput").ap())
    args.append(nc.dram_tensor("out_0", (rows, hid), _mybir.dt.float32, kind="ExternalOutput").ap())
    gated_recurrence(nc, *args)
    r = _run(nc, [arrays], core_ids=[0])
    return r.results[0]["out_0"]
```

```python
import concourse.bass as bass
from concourse import mybir
from contextlib import ExitStack


def gated_recurrence(nc, state_cols, token, gates_first, gates_mid, gates_late, weights, out):
    fp32, fp16 = mybir.dt.float32, mybir.dt.float16
    i32, u32 = mybir.dt.int32, mybir.dt.uint32
    ALU = mybir.AluOpType
    ACT = mybir.ActivationFunctionType

    P = 128
    HID, ROWS = state_cols.shape
    LAYERS = weights.shape[0]
    VOCAB = gates_mid.shape[0]
    TILES = ROWS // P
    PAIR = 2
    PAIRS = TILES // PAIR
    KC = HID // P
    WIDE = PAIR * HID
    CHUNKS = [(0, 1), (1, 3), (3, LAYERS)]
    TABLES = [gates_first, gates_mid, gates_late]
    LAST = LAYERS - 1
    LOOPS = [(1, 3), (3, LAST)]
    LAG = 4
    NU = 8
    PRODUCT_BANK = [q % 2 for q in range(PAIRS)]
    TURNED_BANK = [q % 4 for q in range(PAIRS)]
    POOL_ADDS = {1: (0,), 3: (1, 3, 5, 7), LAST: (0, 2, 4, 6)}
    GATHERED = {1: 4, 2: 2}
    WARM = 9
    AHEAD = 3
    SUM_AT = {1: 0, 2: 1, 3: 2, 4: 3, 5: 4}
    SCALES_AT = {3: (0, 0, 1), 7: (1, 1, LAYERS - 1)}
    HEAD_AT, REST_AT = 4, 5
    SPLIT = LAYERS - 1
    TOP = 14
    STATE_SCALE = float(2 ** 15)
    MANTISSA, BIAS = 23, 127

    def pool_adds(layer):
        since = [first for first in POOL_ADDS if first <= layer]
        return POOL_ADDS[max(since)] if since else ()

    with ExitStack() as ctx:
        def sb(name, shape, dt):
            return ctx.enter_context(nc.sbuf_tensor(name, shape, dt))

        def sem(name):
            return ctx.enter_context(nc.semaphore(name))

        state = sb("state", [P, TILES, HID], fp32)
        first_cols = sb("first_cols", [P, KC, ROWS], fp32)
        head = sb("head", [P, PAIRS, KC, PAIR * P], fp16)
        rest = sb("rest", [P, PAIRS, KC, PAIR * P], fp16)
        gates = sb("gates", [P, TILES, LAYERS, HID], fp32)
        sums = sb("sums", [P, NU, PAIR, HID], fp32)
        w_full = sb("w_full", [P, LAYERS, KC * HID], fp32)
        w_head = sb("w_head", [P, SPLIT, KC * HID], fp16)
        w_rest = sb("w_rest", [P, SPLIT, KC * HID], fp16)
        w_abs = sb("w_abs", [P, KC * HID], fp32)
        w_sum = sb("w_sum", [P, SPLIT], fp32)
        w_total = sb("w_total", [P, SPLIT], fp32)
        w_expo = sb("w_expo", [P, SPLIT], i32)
        w_up = sb("w_up", [P, SPLIT], i32)
        w_down = sb("w_down", [P, SPLIT], i32)
        ones = sb("ones", [P, P], fp32)
        ident = sb("ident", [P, P], fp32)
        tok = sb("tok", [P, TILES], i32)
        wrap = sb("wrap", [P, TILES], fp32)
        tok_wrapped = sb("tok_wrapped", [P, TILES], fp32)
        index = sb("index", [P, TILES], u32)

        products = [ctx.enter_context(nc.psum_tensor(f"products{i}", [P, PAIR, HID], fp32)) for i in range(max(PRODUCT_BANK) + 1)]
        turned = [ctx.enter_context(nc.psum_tensor(f"turned{i}", [P, KC, PAIR * P], fp32)) for i in range(max(TURNED_BANK) + 1)]
        first_rows = ctx.enter_context(nc.psum_tensor("first_rows", [P, PAIR, HID], fp32))
        totals = ctx.enter_context(nc.psum_tensor("totals", [P, P], fp32))

        tok_in = sem("tok_in")
        w_in = [sem(f"w_in{l}") for l in range(LAYERS)]
        cols_in = [sem(f"cols_in{q}") for q in range(PAIRS)]
        rows_ready = sem("rows_ready")
        gates_in = [[sem(f"gates{c}_in{q}") for q in range(PAIRS)] for c in range(len(CHUNKS))]
        ident_zero = sem("ident_zero")
        ident_ready = sem("ident_ready")
        ones_ready = sem("ones_ready")
        index_steps = sem("index_steps")
        scale_steps = sem("scale_steps")
        w_sum_ready = sem("w_sum_ready")
        total_ready = sem("total_ready")
        w_head_ready = sem("w_head_ready")
        w_rest_ready = sem("w_rest_ready")
        product_ready = sem("product_ready")
        gated_ready = sem("gated_ready")
        vector_added = sem("vector_added")
        pool_added = sem("pool_added")
        state_ready = sem("state_ready")
        turned_ready = sem("turned_ready")
        head_ready = sem("head_ready")
        rest_ready = sem("rest_ready")
        stored = sem("stored")

        INDEX_STEPS = 3
        SCALE_STEPS = 4

        def since_bank(banks, q):
            return next(n for n in range(1, PAIRS + 1) if banks[(q - n) % PAIRS] == banks[q])

        def pair_rows(t, q):
            return t[:, PAIR * q:PAIR * (q + 1), :]

        block = ctx.enter_context(nc.Block())

        def w_parts(l):
            cut = bass.ds(l * (KC * HID), KC * HID)
            whole = w_full[:, 1:, :].rearrange("p l n -> p (l n)")[:, cut]
            return (whole, lambda w: w[:, :, :].rearrange("p l n -> p (l n)")[:, cut],
                    w_up[:, :].bitcast(fp32)[:, bass.ds(l, 1)])

        class Layer:
            def __init__(self, at, low):
                self.at, self.low = at, low

            def count(self, per_layer, before):
                return self.at * per_layer + before

            def adds(self, q, pool):
                def made(l, upto=PAIRS):
                    return sum((p in pool_adds(l)) == pool for p in range(upto))
                base = sum(made(l) for l in range(self.low))
                here = made(self.low, q + 1)
                if isinstance(self.at, int):
                    return base + here
                return self.at * made(self.low) + (base - self.low * made(self.low) + here)

        def layers(eng, step):
            step(Layer(0, 0))
            for lo, hi in LOOPS:
                with eng.Fori(lo, hi) as at:
                    step(Layer(at, lo))
            step(Layer(LAST, LAST))

        @block.sync
        def _(sp):
            sp.dma_start(tok[:, :], token.rearrange("(p t) -> p t", t=TILES)).then_inc(tok_in, 16)
            cols_v = state_cols.rearrange("(c k) r -> k c r", c=KC)
            def load_cols(q):
                cols = slice(q * PAIR * P, (q + 1) * PAIR * P)
                sp.dma_start(first_cols[:, :, cols], cols_v[:, :, cols]).then_inc(cols_in[q], 16)

            def load_weights(l):
                sp.dma_start(w_full[:, l, :].rearrange("p (c n) -> p c n", c=KC),
                             weights[l].rearrange("(c p) n -> p c n", c=KC)).then_inc(w_in[l], 16)

            load_cols(0)
            load_weights(0)
            for q in range(1, AHEAD):
                load_cols(q)
            load_weights(1)
            for q in range(AHEAD, PAIRS):
                sp.wait_ge(product_ready, q - AHEAD + 1)
                load_cols(q)
                if q - AHEAD + 2 < LAYERS:
                    load_weights(q - AHEAD + 2)
            out_v = out.rearrange("(p t) h -> p t h", t=TILES)
            for q in range(PAIRS):
                sp.wait_ge(state_ready, LAST * PAIRS + q + 1)
                sp.dma_start(pair_rows(out_v, q), pair_rows(state, q)).then_inc(stored, 16)
            sp.wait_ge(stored, 16 * PAIRS)

        @block.gpsimd
        def _(pool):
            nc.gpsimd.memset(ident[:, :], 0.0).then_inc(ident_zero, 1)
            pool.wait_ge(ident_zero, 1)
            nc.gpsimd.affine_select(out=ident[:, :], in_=ident[:, :], compare_op=ALU.not_equal, fill=1.0,
                                    base=0, pattern=[[-1, P]], channel_multiplier=1).then_inc(ident_ready, 1)
            pool.wait_ge(index_steps, INDEX_STEPS)

            def gather(c, pairs):
                lo, hi = CHUNKS[c]
                for t in range(PAIR * pairs.start, PAIR * pairs.stop):
                    pool.indirect_dma_start(
                        gates[:, t, lo:hi, :].rearrange("p l h -> p (l h)"), None, TABLES[c],
                        bass.IndirectOffsetOnAxis(ap=index[:, t:t + 1], axis=0),
                    ).then_inc(gates_in[c][t // PAIR], 16)

            def add_states(layer):
                for q in pool_adds(layer.low):
                    pool.wait_ge(gated_ready, layer.count(PAIRS, q + 1))
                    nc.gpsimd.tensor_tensor(sums[:, q % NU], sums[:, q % NU], pair_rows(state, q),
                                            ALU.add).then_inc(pool_added, 1)

            gather(0, range(PAIRS))
            for l, pairs in GATHERED.items():
                gather(l, range(pairs))
                add_states(Layer(l, LOOPS[0][0]))
                gather(l, range(pairs, PAIRS))
            with pool.Fori(*LOOPS[1]) as at:
                add_states(Layer(at, LOOPS[1][0]))
            add_states(Layer(LAST, LAST))

        @block.tensor
        def _(pe):
            def product(layer, q):
                bank = products[PRODUCT_BANK[q]]
                if layer.low == 0:
                    pe.wait_ge(cols_in[q], 16)
                    if q == 0:
                        pe.wait_ge(w_in[0], 16)
                else:
                    pe.wait_ge(rest_ready, layer.count(PAIRS, q + 1 - PAIRS))
                if layer.low > 0 and q == 0:
                    pe.wait_ge(w_rest_ready, layer.count(1, 0))
                last_user = since_bank(PRODUCT_BANK, q)
                if layer.low > 0 or q >= last_user:
                    pe.wait_ge(gated_ready, layer.count(PAIRS, q + 1 - last_user))
                for j in range(PAIR):
                    if layer.low == 0:
                        for k in range(KC):
                            cols = (PAIR * q + j) * P
                            last = nc.tensor.matmul(bank[:, j, :], first_cols[:, k, cols:cols + P],
                                                    w_full[:, 0, k * HID:(k + 1) * HID],
                                                    start=(k == 0), stop=(k == KC - 1))
                        continue
                    terms = [(s, w, k) for k in range(KC) for s, w in ((head, w_head), (head, w_rest), (rest, w_head))]
                    for n, (s, w, k) in enumerate(terms):
                        cut = bass.ds((layer.at - 1) * (KC * HID) + k * HID, HID)
                        last = nc.tensor.matmul(bank[:, j, :], s[:, q, k, j * P:(j + 1) * P],
                                                w[:, :, :].rearrange("p l n -> p (l n)")[:, cut],
                                                start=(n == 0), stop=(n == len(terms) - 1))
                last.then_inc(product_ready, 1)

            def turn(layer, q):
                pe.wait_ge(state_ready, layer.count(PAIRS, q + 1))
                last_user = since_bank(TURNED_BANK, q)
                if layer.low > 0 or q >= last_user:
                    pe.wait_ge(rest_ready, layer.count(PAIRS, q + 1 - last_user))
                for j in range(PAIR):
                    for k in range(KC):
                        last = nc.tensor.transpose(turned[TURNED_BANK[q]][:, k, j * P:(j + 1) * P],
                                                   state[:, PAIR * q + j, k * P:(k + 1) * P], ident[:, :])
                last.then_inc(turned_ready, 1)

            def turn_first(q):
                if q >= 1:
                    pe.wait_ge(vector_added, q)
                for j in range(PAIR):
                    for k in range(KC):
                        cols = (PAIR * q + j) * P
                        last = nc.tensor.transpose(first_rows[:, j, k * P:(k + 1) * P],
                                                   first_cols[:, k, cols:cols + P], ident[:, :])
                last.then_inc(rows_ready, 1)

            pe.wait_ge(ones_ready, 1)
            for _ in range(WARM):
                nc.tensor.matmul(totals[:, :], ones[:, :], ones[:, :], start=True, stop=True)
            pe.wait_ge(ident_ready, 1)

            def step(layer):
                for q in range(PAIRS):
                    product(layer, q)
                    if layer.low == 0:
                        turn_first(q)
                    if q >= LAG and layer.low < LAST:
                        turn(layer, q - LAG)
                    elif q < LAG and layer.low > 0:
                        turn(Layer(layer.at - 1, max(layer.low - 1, 0)), PAIRS + q - LAG)
                    if layer.low == 0 and q in SCALES_AT:
                        _, lo, hi = SCALES_AT[q]
                        pe.wait_ge(w_sum_ready, hi)
                        nc.tensor.matmul(totals[:, lo:hi], ones[:, :], w_sum[:, lo:hi],
                                         start=True, stop=True).then_inc(total_ready, 1)

            layers(pe, step)

        @block.scalar
        def _(act):
            def make_head(layer, q):
                act.wait_ge(turned_ready, layer.count(PAIRS, q + 1))
                nc.scalar.activation(head[:, q], turned[TURNED_BANK[q]][:, :, :], ACT.Copy,
                                     scale=STATE_SCALE).then_inc(head_ready, 1)

            def w_make_head(l):
                full, part, up = w_parts(l)
                nc.scalar.activation(part(w_head), full, ACT.Copy, scale=up).then_inc(w_head_ready, 1)

            def new_state(layer, q):
                if q in pool_adds(layer.low):
                    act.wait_ge(pool_added, layer.adds(q, True))
                else:
                    act.wait_ge(vector_added, layer.adds(q, False))
                nc.scalar.activation(pair_rows(state, q), sums[:, q % NU], ACT.Tanh).then_inc(state_ready, 1)

            def step(layer):
                for q in range(PAIRS):
                    if q >= LAG and layer.low < LAST:
                        make_head(layer, q - LAG)
                    elif q < LAG and layer.low > 0:
                        make_head(Layer(layer.at - 1, max(layer.low - 1, 0)), PAIRS + q - LAG)
                    new_state(layer, q)
                    if layer.low == 0 and q in SUM_AT:
                        l = SUM_AT[q]
                        act.wait_ge(w_in[1 + l], 16)
                        if l >= 1:
                            act.wait_ge(w_sum_ready, l)
                        nc.scalar.activation(w_abs[:, :], w_full[:, 1 + l, :], ACT.Abs,
                                             accum_out=w_sum[:, l:l + 1]).then_inc(w_sum_ready, 1)
                    if layer.low < LAST and q == HEAD_AT:
                        act.wait_ge(scale_steps, (1 if layer.low == 0 else 2) * SCALE_STEPS)
                        w_make_head(layer.at)

            layers(act, step)

        @block.vector
        def _(dve):
            nc.vector.memset(ones[:, :], 1.0).then_inc(ones_ready, 1)
            dve.wait_ge(tok_in, 16)
            nc.vector.tensor_scalar(wrap[:, :], tok[:, :], 0.0, float(VOCAB), ALU.is_lt,
                                    ALU.mult).then_inc(index_steps, 1)
            dve.wait_ge(index_steps, 1)
            nc.vector.tensor_tensor(tok_wrapped[:, :], tok[:, :], wrap[:, :], ALU.add).then_inc(index_steps, 1)
            dve.wait_ge(index_steps, 2)
            nc.vector.tensor_scalar(index[:, :], tok_wrapped[:, :], 0.0, float(VOCAB - 1), ALU.max,
                                    ALU.min).then_inc(index_steps, 1)

            def gated(layer, q):
                dve.wait_ge(product_ready, layer.count(PAIRS, q + 1))
                chunk = [c for c, (lo, hi) in enumerate(CHUNKS) if lo <= layer.low < hi][0]
                dve.wait_ge(gates_in[chunk][q], 16 * PAIR)
                if layer.low > 0 or q >= NU:
                    dve.wait_ge(state_ready, layer.count(PAIRS, q + 1 - NU))
                g = gates[:, PAIR * q:PAIR * (q + 1), layer.at, :] if isinstance(layer.at, int) else \
                    gates[:, PAIR * q:PAIR * (q + 1), :, :].rearrange("p t l h -> p t (l h)")[:, :, bass.ds(layer.at * HID, HID)]
                if layer.low == 0:
                    nc.vector.tensor_tensor(sums[:, q % NU], products[PRODUCT_BANK[q]][:, :, :], g,
                                            ALU.mult).then_inc(gated_ready, 1)
                else:
                    down = w_down[:, :].bitcast(fp32)[:, bass.ds(layer.at - 1, 1)]
                    nc.vector.scalar_tensor_tensor(out=sums[:, q % NU], in0=products[PRODUCT_BANK[q]][:, :, :], scalar=down,
                                                   in1=g, op0=ALU.mult, op1=ALU.mult).then_inc(gated_ready, 1)

            def add_state(layer, q):
                dve.wait_ge(gated_ready, layer.count(PAIRS, q + 1))
                if layer.low == 0:
                    dve.wait_ge(rows_ready, q + 1)
                old = first_rows[:, :, :] if layer.low == 0 else pair_rows(state, q)
                nc.vector.tensor_tensor(sums[:, q % NU], sums[:, q % NU], old, ALU.add).then_inc(vector_added, 1)

            def make_rest(layer, q):
                dve.wait_ge(head_ready, layer.count(PAIRS, q + 1))
                nc.vector.scalar_tensor_tensor(out=rest[:, q], in0=turned[TURNED_BANK[q]][:, :, :], scalar=STATE_SCALE,
                                               in1=head[:, q], op0=ALU.mult,
                                               op1=ALU.subtract).then_inc(rest_ready, 1)

            def w_make_rest(l):
                dve.wait_ge(w_head_ready, l + 1)
                full, part, up = w_parts(l)
                nc.vector.scalar_tensor_tensor(out=part(w_rest), in0=full, scalar=up, in1=part(w_head),
                                               op0=ALU.mult, op1=ALU.subtract).then_inc(w_rest_ready, 1)

            REST_LAG = LAG + 1

            def scales(group, lo, hi):
                done = group * SCALE_STEPS
                dve.wait_ge(total_ready, group + 1)
                nc.vector.tensor_scalar(w_total[:, lo:hi], totals[:, lo:hi], 2.0 ** -90, None,
                                        ALU.max).then_inc(scale_steps, 1)
                dve.wait_ge(scale_steps, done + 1)
                nc.vector.tensor_scalar(w_expo[:, lo:hi], w_total[:, lo:hi].bitcast(i32), 0x7F800000, None,
                                        ALU.bitwise_and).then_inc(scale_steps, 1)
                dve.wait_ge(scale_steps, done + 2)
                nc.vector.tensor_scalar(w_up[:, lo:hi], w_expo[:, lo:hi], -1.0,
                                        float((2 * BIAS + TOP) << MANTISSA),
                                        ALU.mult, ALU.add).then_inc(scale_steps, 1)
                nc.vector.tensor_scalar(w_down[:, lo:hi], w_expo[:, lo:hi], -float((TOP + 15) << MANTISSA), None,
                                        ALU.add).then_inc(scale_steps, 1)

            def step(layer):
                for q in range(PAIRS):
                    gated(layer, q)
                    if q >= REST_LAG and layer.low < LAST:
                        make_rest(layer, q - REST_LAG)
                    elif q < REST_LAG and layer.low > 0:
                        make_rest(Layer(layer.at - 1, max(layer.low - 1, 0)), PAIRS + q - REST_LAG)
                    if q not in pool_adds(layer.low):
                        add_state(layer, q)
                    if layer.low == 0 and q in SCALES_AT:
                        scales(*SCALES_AT[q])
                    if layer.low < LAST and q == REST_AT:
                        w_make_rest(layer.at)

            layers(dve, step)


def kernel(**inputs):
    import numpy as _np
    import concourse.bacc as _bacc
    from concourse import mybir as _mybir
    from concourse.bass_utils import run_bass_kernel_spmd as _run

    state = _np.asarray(inputs["r_state"])
    token = _np.asarray(inputs["r_token"])
    ih = _np.asarray(inputs["L0_rec_ih"])
    hh = _np.asarray(inputs["L0_rec_hh"])
    rows, hid = state.shape
    layers, vocab, _ = ih.shape

    def together(lo, hi):
        return ih[lo:hi].transpose(1, 0, 2).reshape(vocab, (hi - lo) * hid)

    host = {
        "state_cols": state.reshape(128, rows // 128, hid).transpose(2, 1, 0).reshape(hid, rows),
        "token": token,
        "gates_first": together(0, 1),
        "gates_mid": together(1, 3),
        "gates_late": together(3, layers),
        "weights": hh,
    }
    nc = _bacc.Bacc("TRN2", target_bir_lowering=False, num_devices=1)
    arrays, args = {}, []
    for name, a in host.items():
        a = _np.ascontiguousarray(a)
        arrays[f"in_{name}"] = a
        args.append(nc.dram_tensor(f"in_{name}", a.shape, _mybir.dt.from_np(a.dtype), kind="ExternalInput").ap())
    args.append(nc.dram_tensor("out_0", (rows, hid), _mybir.dt.float32, kind="ExternalOutput").ap())
    gated_recurrence(nc, *args)
    r = _run(nc, [arrays], core_ids=[0])
    return r.results[0]["out_0"]
```

```python
import concourse.bass as bass
from concourse import mybir
from contextlib import ExitStack


def gated_recurrence(nc, state_cols, token, gates_first, gates_mid, gates_late, weights, out):
    fp32, fp16 = mybir.dt.float32, mybir.dt.float16
    i32, u32 = mybir.dt.int32, mybir.dt.uint32
    ALU = mybir.AluOpType
    ACT = mybir.ActivationFunctionType

    P = 128
    HID, ROWS = state_cols.shape
    LAYERS = weights.shape[0]
    VOCAB = gates_mid.shape[0]
    TILES = ROWS // P
    PAIR = 2
    PAIRS = TILES // PAIR
    KC = HID // P
    CHUNKS = [(0, 1), (1, 3), (3, LAYERS)]
    TABLES = [gates_first, gates_mid, gates_late]
    LAST = LAYERS - 1
    LOOP = (1, 3)
    DMA_TURNS = 3
    TURN_LAG = (3, None)
    HEAD_LAG = (3, 1)
    REST_LAG = (4, 3)
    PRODUCT_BANK = [q % 2 for q in range(PAIRS)]
    TURNED_BANK = [q % 4 for q in range(PAIRS)]
    POOL_ADDS = {1: (6, 7), 3: (2, 3, 4, 5, 6, 7), 4: (0, 1, 2, 3, 4, 5, 6, 7), LAST: (0, 1, 2, 3, 5)}
    GATHERED = {1: (8, 8), 2: (6, 6)}
    WARM = 9
    AHEAD = 3
    SUM_AT = {1: 0, 2: 1, 3: 2, 4: 3, 5: 4}
    SCALES_AT = {3: (0, 0, 1), 7: (1, 1, LAYERS - 1)}
    HEAD_AT, REST_AT = 3, 5
    SPLIT = LAYERS - 1
    TOP = 14
    STATE_SCALE = float(2 ** 15)
    MANTISSA, BIAS = 23, 127

    def pool_adds(layer):
        since = [first for first in POOL_ADDS if first <= layer]
        return POOL_ADDS[max(since)] if since else ()

    with ExitStack() as ctx:
        def sb(name, shape, dt):
            return ctx.enter_context(nc.sbuf_tensor(name, shape, dt))

        def sem(name):
            return ctx.enter_context(nc.semaphore(name))

        state = sb("state", [P, TILES, HID], fp32)
        first_cols = sb("first_cols", [P, KC, ROWS], fp32)
        split_cols = sb("split_cols", [P, PAIRS, 2, PAIR, KC, P], fp16)
        split_rows = sb("split_rows", [P, PAIRS, 2, PAIR, HID], fp16)
        gates = sb("gates", [P, TILES, LAYERS, HID], fp32)
        sums = sb("sums", [P, PAIRS, PAIR, HID], fp32)
        w_full = sb("w_full", [P, LAYERS, KC * HID], fp32)
        w_head = sb("w_head", [P, SPLIT, KC * HID], fp16)
        w_rest = sb("w_rest", [P, SPLIT, KC * HID], fp16)
        w_abs = sb("w_abs", [P, KC * HID], fp32)
        w_sum = sb("w_sum", [P, SPLIT], fp32)
        w_total = sb("w_total", [P, SPLIT], fp32)
        w_expo = sb("w_expo", [P, SPLIT], i32)
        w_up = sb("w_up", [P, SPLIT], i32)
        w_down = sb("w_down", [P, SPLIT], i32)
        ones = sb("ones", [P, P], fp32)
        ident = sb("ident", [P, P], fp32)
        tok = sb("tok", [P, TILES], i32)
        wrap = sb("wrap", [P, TILES], fp32)
        tok_wrapped = sb("tok_wrapped", [P, TILES], fp32)
        index = sb("index", [P, TILES], u32)

        products = [ctx.enter_context(nc.psum_tensor(f"products{i}", [P, PAIR, HID], fp32)) for i in range(max(PRODUCT_BANK) + 1)]
        turned = [ctx.enter_context(nc.psum_tensor(f"turned{i}", [P, PAIR, KC, P], fp32)) for i in range(max(TURNED_BANK) + 1)]
        first_rows = ctx.enter_context(nc.psum_tensor("first_rows", [P, PAIR, HID], fp32))
        totals = ctx.enter_context(nc.psum_tensor("totals", [P, P], fp32))

        tok_in = sem("tok_in")
        w_in = [sem(f"w_in{l}") for l in range(LAYERS)]
        cols_in = [sem(f"cols_in{q}") for q in range(PAIRS)]
        rows_ready = sem("rows_ready")
        gates_in = [[sem(f"gates{c}_in{q}") for q in range(PAIRS)] for c in range(len(CHUNKS))]
        ident_zero = sem("ident_zero")
        ident_ready = sem("ident_ready")
        ones_ready = sem("ones_ready")
        index_steps = sem("index_steps")
        scale_steps = sem("scale_steps")
        w_sum_ready = sem("w_sum_ready")
        total_ready = sem("total_ready")
        w_head_ready = sem("w_head_ready")
        w_rest_ready = sem("w_rest_ready")
        product_ready = sem("product_ready")
        gated_ready = sem("gated_ready")
        vector_added = sem("vector_added")
        pool_added = sem("pool_added")
        state_ready = sem("state_ready")
        turned_ready = sem("turned_ready")
        turned_in = [sem(f"turned{q}_in") for q in range(PAIRS)]
        head_ready = sem("head_ready")
        rest_ready = sem("rest_ready")
        head_rows_ready = sem("head_rows_ready")
        rest_rows_ready = sem("rest_rows_ready")
        stored = sem("stored")

        INDEX_STEPS = 3
        SCALE_STEPS = 4

        def since_bank(banks, q):
            return next(n for n in range(1, PAIRS + 1) if banks[(q - n) % PAIRS] == banks[q])

        def pair_rows(t, q):
            return t[:, PAIR * q:PAIR * (q + 1), :]

        def cuts(layer, q):
            if layer.low == LAST and q == PAIRS - 1:
                return [slice(j, j + 1) for j in range(PAIR)]
            return [slice(0, PAIR)]

        def product_bank(layer, q, cut):
            return first_rows if len(cuts(layer, q)) > 1 and cut.start > 0 else products[PRODUCT_BANK[q]]

        def by_dma(l):
            return int(l >= DMA_TURNS)

        def due(layer, q, lags):
            lag = lags[by_dma(layer.low)]
            if layer.low < LAST and lag is not None and q >= lag:
                yield layer, q - lag
            if layer.low > 0:
                before = Layer(layer.at - 1, max(layer.low - 1, 0))
                lag = lags[by_dma(before.low)]
                if lag is not None and q < lag:
                    yield before, PAIRS + q - lag

        block = ctx.enter_context(nc.Block())

        def w_parts(l):
            cut = bass.ds(l * (KC * HID), KC * HID)
            whole = w_full[:, 1:, :].rearrange("p l n -> p (l n)")[:, cut]
            return (whole, lambda w: w[:, :, :].rearrange("p l n -> p (l n)")[:, cut],
                    w_up[:, :].bitcast(fp32)[:, bass.ds(l, 1)])

        class Layer:
            def __init__(self, at, low):
                self.at, self.low = at, low

            def count(self, per_layer, before):
                return self.at * per_layer + before

            def adds(self, q, pool):
                def made(l, upto=PAIRS):
                    return sum((p in pool_adds(l)) == pool for p in range(upto))
                base = sum(made(l) for l in range(self.low))
                here = made(self.low, q + 1)
                if isinstance(self.at, int):
                    return base + here
                return self.at * made(self.low) + (base - self.low * made(self.low) + here)

        def layers(eng, step):
            lo, hi = LOOP
            for l in range(lo):
                step(Layer(l, l))
            with eng.Fori(lo, hi) as at:
                step(Layer(at, lo))
            for l in range(hi, LAYERS):
                step(Layer(l, l))

        @block.sync
        def _(sp):
            sp.dma_start(tok[:, :], token.rearrange("(p t) -> p t", t=TILES)).then_inc(tok_in, 16)
            cols_v = state_cols.rearrange("(c k) r -> k c r", c=KC)
            def load_cols(q):
                cols = slice(q * PAIR * P, (q + 1) * PAIR * P)
                sp.dma_start(first_cols[:, :, cols], cols_v[:, :, cols]).then_inc(cols_in[q], 16)

            def load_weights(l):
                sp.dma_start(w_full[:, l, :].rearrange("p (c n) -> p c n", c=KC),
                             weights[l].rearrange("(c p) n -> p c n", c=KC)).then_inc(w_in[l], 16)

            load_cols(0)
            load_weights(0)
            for q in range(1, AHEAD):
                load_cols(q)
            load_weights(1)
            for q in range(AHEAD, PAIRS):
                sp.wait_ge(product_ready, q - AHEAD + 1)
                load_cols(q)
                if q - AHEAD + 2 < LAYERS:
                    load_weights(q - AHEAD + 2)
            for l in range(DMA_TURNS, LAST):
                for q in range(PAIRS):
                    sp.wait_ge(rest_rows_ready, (l - DMA_TURNS) * PAIRS + q + 1)
                    sp.dma_start_transpose(split_cols[:, q].rearrange("p s j k r -> p (s j k) r"),
                                           split_rows[:, q].rearrange("p s j n -> p (s j n)")).then_inc(turned_in[q], 16)
            out_v = out.rearrange("(p t) h -> p t h", t=TILES)
            stores = 0
            for q in range(PAIRS):
                for cut in cuts(Layer(LAST, LAST), q):
                    stores += 1
                    sp.wait_ge(state_ready, LAST * PAIRS + stores)
                    sp.dma_start(pair_rows(out_v, q)[:, cut], pair_rows(state, q)[:, cut]).then_inc(stored, 16)
            sp.wait_ge(stored, 16 * stores)

        @block.gpsimd
        def _(pool):
            nc.gpsimd.memset(ident[:, :], 0.0).then_inc(ident_zero, 1)
            pool.wait_ge(ident_zero, 1)
            nc.gpsimd.affine_select(out=ident[:, :], in_=ident[:, :], compare_op=ALU.not_equal, fill=1.0,
                                    base=0, pattern=[[-1, P]], channel_multiplier=1).then_inc(ident_ready, 1)
            pool.wait_ge(index_steps, INDEX_STEPS)

            def gather(c, pairs):
                lo, hi = CHUNKS[c]
                for t in range(PAIR * pairs.start, PAIR * pairs.stop):
                    pool.indirect_dma_start(
                        gates[:, t, lo:hi, :].rearrange("p l h -> p (l h)"), None, TABLES[c],
                        bass.IndirectOffsetOnAxis(ap=index[:, t:t + 1], axis=0),
                    ).then_inc(gates_in[c][t // PAIR], 16)

            def add_state(layer, q):
                pool.wait_ge(gated_ready, layer.count(PAIRS, q + 1))
                nc.gpsimd.tensor_tensor(sums[:, q], sums[:, q], pair_rows(state, q),
                                        ALU.add).then_inc(pool_added, 1)

            gather(0, range(PAIRS))
            for l in range(*LOOP):
                done = 0
                for q, pairs in zip(pool_adds(l), GATHERED[l]):
                    gather(l, range(done, pairs))
                    add_state(Layer(l, l), q)
                    done = pairs
                gather(l, range(done, PAIRS))
            for l in range(LOOP[1], LAYERS):
                for q in pool_adds(l):
                    add_state(Layer(l, l), q)

        @block.tensor
        def _(pe):
            def product(layer, q):
                if layer.low == 0:
                    pe.wait_ge(cols_in[q], 16)
                    if q == 0:
                        pe.wait_ge(w_in[0], 16)
                elif by_dma(layer.low - 1):
                    pe.wait_ge(turned_in[q], 16 * (layer.at - DMA_TURNS))
                else:
                    pe.wait_ge(rest_ready, layer.count(PAIRS, q + 1 - PAIRS))
                if layer.low > 0 and q == 0:
                    pe.wait_ge(w_rest_ready, layer.count(1, 0))
                last_user = since_bank(PRODUCT_BANK, q)
                if layer.low > 0 or q >= last_user:
                    pe.wait_ge(gated_ready, layer.count(PAIRS, q + 1 - last_user))
                for cut in cuts(layer, q):
                    bank = product_bank(layer, q, cut)
                    for j in range(cut.start, cut.stop):
                        last = tile_product(layer, q, j, bank)
                    last.then_inc(product_ready, 1)

            def tile_product(layer, q, j, bank):
                if layer.low == 0:
                    for k in range(KC):
                        cols = (PAIR * q + j) * P
                        last = nc.tensor.matmul(bank[:, j, :], first_cols[:, k, cols:cols + P],
                                                w_full[:, 0, k * HID:(k + 1) * HID],
                                                start=(k == 0), stop=(k == KC - 1))
                    return last
                terms = [(s, w, k) for k in range(KC) for s, w in ((0, w_head), (0, w_rest), (1, w_head))]
                for n, (s, w, k) in enumerate(terms):
                    cut = bass.ds((layer.at - 1) * (KC * HID) + k * HID, HID)
                    last = nc.tensor.matmul(bank[:, j, :], split_cols[:, q, s, j, k, :],
                                            w[:, :, :].rearrange("p l n -> p (l n)")[:, cut],
                                            start=(n == 0), stop=(n == len(terms) - 1))
                return last

            def turn(layer, q):
                pe.wait_ge(state_ready, layer.count(PAIRS, q + 1))
                last_user = since_bank(TURNED_BANK, q)
                if layer.low > 0 or q >= last_user:
                    pe.wait_ge(rest_ready, layer.count(PAIRS, q + 1 - last_user))
                for j in range(PAIR):
                    for k in range(KC):
                        last = nc.tensor.transpose(turned[TURNED_BANK[q]][:, j, k, :],
                                                   state[:, PAIR * q + j, k * P:(k + 1) * P], ident[:, :])
                last.then_inc(turned_ready, 1)

            def turn_first(q):
                if q >= 1:
                    pe.wait_ge(vector_added, q)
                for j in range(PAIR):
                    for k in range(KC):
                        cols = (PAIR * q + j) * P
                        last = nc.tensor.transpose(first_rows[:, j, k * P:(k + 1) * P],
                                                   first_cols[:, k, cols:cols + P], ident[:, :])
                last.then_inc(rows_ready, 1)

            pe.wait_ge(ones_ready, 1)
            for _ in range(WARM):
                nc.tensor.matmul(totals[:, :], ones[:, :], ones[:, :], start=True, stop=True)
            pe.wait_ge(ident_ready, 1)

            def step(layer):
                for q in range(PAIRS):
                    product(layer, q)
                    if layer.low == 0:
                        turn_first(q)
                    for of, pair in due(layer, q, TURN_LAG):
                        turn(of, pair)
                    if layer.low == 0 and q in SCALES_AT:
                        _, lo, hi = SCALES_AT[q]
                        pe.wait_ge(w_sum_ready, hi)
                        nc.tensor.matmul(totals[:, lo:hi], ones[:, :], w_sum[:, lo:hi],
                                         start=True, stop=True).then_inc(total_ready, 1)

            layers(pe, step)

        @block.scalar
        def _(act):
            def make_head(layer, q):
                if by_dma(layer.low):
                    act.wait_ge(state_ready, layer.count(PAIRS, q + 1))
                    nc.scalar.activation(split_rows[:, q, 0], pair_rows(state, q), ACT.Copy,
                                         scale=STATE_SCALE).then_inc(head_rows_ready, 1)
                else:
                    act.wait_ge(turned_ready, layer.count(PAIRS, q + 1))
                    nc.scalar.activation(split_cols[:, q, 0], turned[TURNED_BANK[q]][:, :, :, :], ACT.Copy,
                                         scale=STATE_SCALE).then_inc(head_ready, 1)

            def w_make_head(l):
                full, part, up = w_parts(l)
                nc.scalar.activation(part(w_head), full, ACT.Copy, scale=up).then_inc(w_head_ready, 1)

            def new_state(layer, q):
                if q in pool_adds(layer.low):
                    act.wait_ge(pool_added, layer.adds(q, True))
                else:
                    act.wait_ge(vector_added, layer.adds(q, False))
                for n, cut in enumerate(cuts(layer, q)):
                    if n >= 1:
                        act.wait_ge(vector_added, layer.adds(q, False) + n)
                    nc.scalar.activation(pair_rows(state, q)[:, cut], sums[:, q, cut], ACT.Tanh).then_inc(state_ready, 1)

            def step(layer):
                for q in range(PAIRS):
                    for of, pair in due(layer, q, HEAD_LAG):
                        make_head(of, pair)
                    new_state(layer, q)
                    if layer.low == 0 and q in SUM_AT:
                        l = SUM_AT[q]
                        act.wait_ge(w_in[1 + l], 16)
                        if l >= 1:
                            act.wait_ge(w_sum_ready, l)
                        nc.scalar.activation(w_abs[:, :], w_full[:, 1 + l, :], ACT.Abs,
                                             accum_out=w_sum[:, l:l + 1]).then_inc(w_sum_ready, 1)
                    if layer.low < LAST and q == HEAD_AT:
                        act.wait_ge(scale_steps, (1 if layer.low == 0 else 2) * SCALE_STEPS)
                        w_make_head(layer.at)

            layers(act, step)

        @block.vector
        def _(dve):
            nc.vector.memset(ones[:, :], 1.0).then_inc(ones_ready, 1)
            dve.wait_ge(tok_in, 16)
            nc.vector.tensor_scalar(wrap[:, :], tok[:, :], 0.0, float(VOCAB), ALU.is_lt,
                                    ALU.mult).then_inc(index_steps, 1)
            dve.wait_ge(index_steps, 1)
            nc.vector.tensor_tensor(tok_wrapped[:, :], tok[:, :], wrap[:, :], ALU.add).then_inc(index_steps, 1)
            dve.wait_ge(index_steps, 2)
            nc.vector.tensor_scalar(index[:, :], tok_wrapped[:, :], 0.0, float(VOCAB - 1), ALU.max,
                                    ALU.min).then_inc(index_steps, 1)

            def gated(layer, q, n, cut):
                dve.wait_ge(product_ready, layer.count(PAIRS, q + 1 + n))
                chunk = [c for c, (lo, hi) in enumerate(CHUNKS) if lo <= layer.low < hi][0]
                dve.wait_ge(gates_in[chunk][q], 16 * PAIR)
                if layer.low > 0:
                    dve.wait_ge(state_ready, layer.count(PAIRS, q + 1 - PAIRS))
                product = product_bank(layer, q, cut)[:, cut]
                if isinstance(layer.at, int):
                    g = pair_rows(gates, q)[:, cut, layer.at, :]
                else:
                    g = pair_rows(gates, q)[:, cut].rearrange("p t l h -> p t (l h)")[:, :, bass.ds(layer.at * HID, HID)]
                if layer.low == 0:
                    nc.vector.tensor_tensor(sums[:, q, cut], product, g, ALU.mult).then_inc(gated_ready, 1)
                else:
                    down = w_down[:, :].bitcast(fp32)[:, bass.ds(layer.at - 1, 1)]
                    nc.vector.scalar_tensor_tensor(out=sums[:, q, cut], in0=product, scalar=down, in1=g,
                                                   op0=ALU.mult, op1=ALU.mult).then_inc(gated_ready, 1)

            def add_state(layer, q, n, cut):
                dve.wait_ge(gated_ready, layer.count(PAIRS, q + 1 + n))
                if layer.low == 0:
                    dve.wait_ge(rows_ready, q + 1)
                old = first_rows[:, :, :] if layer.low == 0 else pair_rows(state, q)
                nc.vector.tensor_tensor(sums[:, q, cut], sums[:, q, cut], old[:, cut], ALU.add).then_inc(vector_added, 1)

            def make_rest(layer, q):
                if by_dma(layer.low):
                    dve.wait_ge(head_rows_ready, (layer.at - DMA_TURNS) * PAIRS + q + 1)
                    nc.vector.scalar_tensor_tensor(out=split_rows[:, q, 1], in0=pair_rows(state, q), scalar=STATE_SCALE,
                                                   in1=split_rows[:, q, 0], op0=ALU.mult,
                                                   op1=ALU.subtract).then_inc(rest_rows_ready, 1)
                else:
                    dve.wait_ge(head_ready, layer.count(PAIRS, q + 1))
                    nc.vector.scalar_tensor_tensor(out=split_cols[:, q, 1], in0=turned[TURNED_BANK[q]][:, :, :, :],
                                                   scalar=STATE_SCALE, in1=split_cols[:, q, 0], op0=ALU.mult,
                                                   op1=ALU.subtract).then_inc(rest_ready, 1)

            def w_make_rest(l):
                dve.wait_ge(w_head_ready, l + 1)
                full, part, up = w_parts(l)
                nc.vector.scalar_tensor_tensor(out=part(w_rest), in0=full, scalar=up, in1=part(w_head),
                                               op0=ALU.mult, op1=ALU.subtract).then_inc(w_rest_ready, 1)

            def scales(group, lo, hi):
                done = group * SCALE_STEPS
                dve.wait_ge(total_ready, group + 1)
                nc.vector.tensor_scalar(w_total[:, lo:hi], totals[:, lo:hi], 2.0 ** -90, None,
                                        ALU.max).then_inc(scale_steps, 1)
                dve.wait_ge(scale_steps, done + 1)
                nc.vector.tensor_scalar(w_expo[:, lo:hi], w_total[:, lo:hi].bitcast(i32), 0x7F800000, None,
                                        ALU.bitwise_and).then_inc(scale_steps, 1)
                dve.wait_ge(scale_steps, done + 2)
                nc.vector.tensor_scalar(w_up[:, lo:hi], w_expo[:, lo:hi], -1.0,
                                        float((2 * BIAS + TOP) << MANTISSA),
                                        ALU.mult, ALU.add).then_inc(scale_steps, 1)
                nc.vector.tensor_scalar(w_down[:, lo:hi], w_expo[:, lo:hi], -float((TOP + 15) << MANTISSA), None,
                                        ALU.add).then_inc(scale_steps, 1)

            def step(layer):
                for q in range(PAIRS):
                    for n, cut in enumerate(cuts(layer, q)):
                        gated(layer, q, n, cut)
                        if n == 0:
                            for of, pair in due(layer, q, REST_LAG):
                                make_rest(of, pair)
                        if q not in pool_adds(layer.low):
                            add_state(layer, q, n, cut)
                    if layer.low == 0 and q in SCALES_AT:
                        scales(*SCALES_AT[q])
                    if layer.low < LAST and q == REST_AT:
                        w_make_rest(layer.at)

            layers(dve, step)


def kernel(**inputs):
    import numpy as _np
    import concourse.bacc as _bacc
    from concourse import mybir as _mybir
    from concourse.bass_utils import run_bass_kernel_spmd as _run

    state = _np.asarray(inputs["r_state"])
    token = _np.asarray(inputs["r_token"])
    ih = _np.asarray(inputs["L0_rec_ih"])
    hh = _np.asarray(inputs["L0_rec_hh"])
    rows, hid = state.shape
    layers, vocab, _ = ih.shape

    def together(lo, hi):
        return ih[lo:hi].transpose(1, 0, 2).reshape(vocab, (hi - lo) * hid)

    host = {
        "state_cols": state.reshape(128, rows // 128, hid).transpose(2, 1, 0).reshape(hid, rows),
        "token": token,
        "gates_first": together(0, 1),
        "gates_mid": together(1, 3),
        "gates_late": together(3, layers),
        "weights": hh,
    }
    nc = _bacc.Bacc("TRN2", target_bir_lowering=False, num_devices=1)
    arrays, args = {}, []
    for name, a in host.items():
        a = _np.ascontiguousarray(a)
        arrays[f"in_{name}"] = a
        args.append(nc.dram_tensor(f"in_{name}", a.shape, _mybir.dt.from_np(a.dtype), kind="ExternalInput").ap())
    args.append(nc.dram_tensor("out_0", (rows, hid), _mybir.dt.float32, kind="ExternalOutput").ap())
    gated_recurrence(nc, *args)
    r = _run(nc, [arrays], core_ids=[0])
    return r.results[0]["out_0"]
```
